# Optimizing a Trainium2 kernel written in Bass

```python
import numpy as np
import jax
import jax.numpy as jnp

def _softmax(x, axis=-1):
    return jax.nn.softmax(x, axis=axis)
def _gelu(x):
    return jax.nn.gelu(x, approximate=True)
def _silu(x):
    return jax.nn.silu(x)
def _sigmoid(x):
    return jax.nn.sigmoid(x)
def _layernorm(x, axis=-1, eps=1e-5):
    m = jnp.mean(x, axis=axis, keepdims=True)
    v = jnp.var(x, axis=axis, keepdims=True)
    return (x - m) / jnp.sqrt(v + eps)
def _scatter_add(tgt, idx, src, axis=0):
    return tgt.at[idx].add(src)
def _segment_sum(src, seg, n):
    return jax.ops.segment_sum(src, seg, n)

kernel_name = 'mk_conv_seq_d1_conv_nchw256_c1ea53'

def setup_inputs(seed: int = 0):
    np.random.seed(seed)
    _w = jnp.asarray
    def _rec_inputs():
        import jax
        import jax.numpy as jnp
        _gk = jax.random.key(seed)
        x = -7.109e-05 + 0.9999 * jax.random.normal(jax.random.fold_in(_gk, 1), (16, 256, 128, 128), jnp.float32)
        return x
    x = _rec_inputs()
    def _L0_conv_setup():
        import jax, jax.numpy as jnp
        import numpy as np
        C = 256
        key = jax.random.key(seed)
        k1, k2, k3, k4, k5 = jax.random.split(key, 5)
        x = jax.random.normal(k1, (16, C, 128, 128), dtype=jnp.float32)
        w1 = jax.random.normal(k2, (C,), dtype=jnp.float32) * (1.0 / np.sqrt(C))
        b1 = jax.random.normal(k3, (), dtype=jnp.float32) * 0.01
        w2 = jax.random.normal(k4, (C, C), dtype=jnp.float32) * (1.0 / np.sqrt(C))
        b2 = jax.random.normal(k5, (C,), dtype=jnp.float32) * 0.01
        return {'x': x, 'w1': w1, 'b1': b1, 'w2': w2, 'b2': b2}
    _L0_conv_all = _L0_conv_setup()
    _L0_conv_in = {k: v for k, v in _L0_conv_all.items() if k in ('w1', 'b1', 'w2', 'b2', )}
    del _L0_conv_all

    return {
        "x": x,
        "L0_conv_w1": _L0_conv_in["w1"],
        "L0_conv_b1": _L0_conv_in["b1"],
        "L0_conv_w2": _L0_conv_in["w2"],
        "L0_conv_b2": _L0_conv_in["b2"],
    }

def reference(x, L0_conv_w1, L0_conv_b1, L0_conv_w2, L0_conv_b2):
    import jax
    import jax.numpy as jnp
    def _L0_conv_ref(x, w1, b1, w2, b2):
        import jax, jax.numpy as jnp
        import numpy as np
        C = 256
        n, c, h, w = x.shape
        xf = x.reshape(n, c, h * w)
        logits = jnp.einsum('ncs,c->ns', xf, w1) + b1
        attn = jax.nn.softmax(logits, axis=-1)
        pooled = jnp.einsum('ncs,ns->nc', xf, attn)
        ctx = jnp.einsum('oc,nc->no', w2, pooled) + b2
        return x + ctx[:, :, None, None]

    def _gn(v, G=32, eps=1e-5):
        B_, C_, H_, W_ = v.shape
        g = v.reshape(B_, G, C_ // G, H_, W_)
        m = jnp.mean(g, axis=(2, 3, 4), keepdims=True)
        s = jnp.var(g, axis=(2, 3, 4), keepdims=True)
        return ((g - m) / jnp.sqrt(s + eps)).reshape(v.shape)

    def _ln_c(v, eps=1e-6):
        m = jnp.mean(v, axis=1, keepdims=True)
        s = jnp.var(v, axis=1, keepdims=True)
        return (v - m) / jnp.sqrt(s + eps)

    def _ln_t(v, eps=1e-5):
        m = jnp.mean(v, axis=-1, keepdims=True)
        s = jnp.var(v, axis=-1, keepdims=True)
        return (v - m) / jnp.sqrt(s + eps)

    def _to_tokens(v):
        B_, C_, H_, W_ = v.shape
        return v.reshape(B_, C_, H_ * W_).transpose(0, 2, 1)
    def _from_tokens(t, like):
        B_, C_, H_, W_ = like.shape
        return t.transpose(0, 2, 1).reshape(B_, C_, H_, W_)

    x = _L0_conv_ref(x, L0_conv_w1, L0_conv_b1, L0_conv_w2, L0_conv_b2)
    return x


_drawn_inputs = setup_inputs


def setup_inputs(seed=0):
    import zlib

    import numpy as np

    out = dict(_drawn_inputs(seed))
    spreads = {}
    factors = {'L0_conv_b2': 5.829}
    for name, (base, spread) in spreads.items():
        noise = np.random.default_rng([zlib.crc32(name.encode()), seed]).standard_normal(out[name].shape)
        drawn = base * np.exp(spread * noise) if base else spread * noise
        out[name] = jnp.asarray(drawn.astype(out[name].dtype))
    for name, factor in factors.items():
        out[name] = (out[name] * factor).astype(out[name].dtype)
    return out
```

```python
import concourse.bass as bass
from concourse import mybir
from contextlib import ExitStack


def context_block_kernel(nc: bass.Bass, x: bass.AP, w1: bass.AP, b1: bass.AP, w2: bass.AP, b2: bass.AP,
                         out: bass.AP):
    F32 = mybir.dt.float32
    BF16 = mybir.dt.bfloat16
    ALU = mybir.AluOpType
    ACT = mybir.ActivationFunctionType
    AX = mybir.AxisListType

    P = 128
    SAMPLES, C, H, W = x.shape
    HALVES = C // P
    CHUNK = 1024
    CHUNKS = H * W // CHUNK
    SLOTS = 24
    AHEAD = SLOTS - CHUNKS
    BANK = 512
    LOGIT_BUFS = 3
    EXP_BUFS = 2
    ROUND = 3
    LAG = 2
    TOTAL = SAMPLES * CHUNKS
    LAST = SAMPLES - 1
    assert (ROUND * CHUNKS) % SLOTS == 0 and (ROUND * CHUNKS) % LOGIT_BUFS == 0
    assert CHUNKS % EXP_BUFS == 0 and LAST % ROUND == 0

    x_v = x.rearrange("n (h p) a b -> p n h (a b)", p=P)
    out_v = out.rearrange("n (h p) a b -> p n h (a b)", p=P)

    with ExitStack() as ctx:
        def sb(name, shape, dt=F32):
            return ctx.enter_context(nc.sbuf_tensor(name, shape, dt))

        def sem(name):
            return ctx.enter_context(nc.semaphore(name))

        xs = sb("xs", [P, SLOTS, HALVES, CHUNK])
        exps = sb("exps", [P, EXP_BUFS, CHUNK])
        products = sb("products", [P, EXP_BUFS, HALVES, CHUNK], BF16)
        w1_cols = sb("w1_cols", [P, HALVES])
        neg_w1 = sb("neg_w1", [P, HALVES, P])
        neg_b1 = sb("neg_b1", [P, 1])
        b2_cols = sb("b2_cols", [P, HALVES])
        w2T = sb("w2T", [P, HALVES, C])
        neg_max = sb("neg_max", [P, ROUND, CHUNKS])
        sums = sb("sums", [P, ROUND, CHUNKS])
        pools = sb("pools", [P, ROUND, HALVES, CHUNKS])
        neg_top = sb("neg_top", [P, ROUND])
        weights = sb("weights", [P, ROUND, CHUNKS])
        weighted = sb("weighted", [P, HALVES + 1, CHUNKS])
        total = sb("total", [P, ROUND])
        inverse = sb("inverse", [P, ROUND])
        pooled = sb("pooled", [P, ROUND, HALVES])
        context = sb("context", [P, ROUND, HALVES])
        w2_rows = xs[:, SLOTS - 1, 0, 0:HALVES * C].rearrange("p (h c) -> p h c", h=HALVES)
        identity = xs[:, SLOTS - 1, 1, 0:P]

        logits = ctx.enter_context(nc.psum_tensor("logits", [P, LOGIT_BUFS, CHUNK], F32))
        transposed = ctx.enter_context(nc.psum_tensor("transposed", [P, HALVES, C], F32))
        mapped = ctx.enter_context(nc.psum_tensor("mapped", [P, BANK], F32))

        w1_loaded = sem("w1_loaded")
        b1_loaded = sem("b1_loaded")
        w2_loaded = sem("w2_loaded")
        b2_loaded = sem("b2_loaded")
        identity_zeroed = sem("identity_zeroed")
        identity_made = sem("identity_made")
        w1_spread = sem("w1_spread")
        w1_ones = sem("w1_ones")
        b1_negated = sem("b1_negated")
        w2_transposed = sem("w2_transposed")
        w2_copied = sem("w2_copied")
        chunk_loaded = [sem(f"chunk_loaded{k}") for k in range(CHUNKS)]
        chunk_stored = [sem(f"chunk_stored{k}") for k in range(CHUNKS)]
        logits_ready = sem("logits_ready")
        min_ready = sem("min_ready")
        exp_ready = sem("exp_ready")
        chunk_pooled = sem("chunk_pooled")
        top_ready = sem("top_ready")
        weights_ready = sem("weights_ready")
        weighted_used = sem("weighted_used")
        total_ready = sem("total_ready")
        inverse_ready = sem("inverse_ready")
        pooled_ready = sem("pooled_ready")
        mapped_ready = sem("mapped_ready")
        context_ready = sem("context_ready")
        chunk_added = [sem(f"chunk_added{k}") for k in range(CHUNKS)]

        block = ctx.enter_context(nc.Block())

        def slot(r, k):
            return (r * CHUNKS + k) % SLOTS

        def wait(eng, semaphore, value):
            if not isinstance(value, int) or value > 0:
                eng.wait_ge(semaphore, value)

        def samples(eng, body):
            body(0, 0)
            with eng.Fori(0, LAST // ROUND) as i:
                for j in range(ROUND):
                    body(i * ROUND + (1 + j), (1 + j) % ROUND)

        @block.sync
        def _(sp):
            def work_out(value):
                if not isinstance(value, int):
                    sp.compute_val(value)
                return value

            def load(n, r, k, loads_before):
                wait(sp, chunk_loaded[k], loads_before)
                sp.dma_start(xs[:, slot(r, k)],
                             x_v[:, bass.ds(n, 1), :, k * CHUNK:(k + 1) * CHUNK]).then_inc(chunk_loaded[k], 16)

            def stores_and_loads(n, r, first=0, end=CHUNKS):
                for m in range(3):
                    work_out((n + m) * (C * H * W) * 4)
                dma_ends = [work_out((n + m) * 16) for m in range(3)]
                added = work_out((n + 1) * 2)
                for k in range(CHUNKS):
                    sp.wait_ge(chunk_added[k], added)
                    sp.dma_start(out_v[:, bass.ds(n, 1), :, k * CHUNK:(k + 1) * CHUNK],
                                 xs[:, slot(r, k)]).then_inc(chunk_stored[k], 16)
                    if first <= k < end:
                        m, q = divmod(k - LAG, CHUNKS)
                        sp.wait_ge(chunk_stored[q], dma_ends[m + 1])
                        up, q = divmod(k - LAG + SLOTS, CHUNKS)
                        load(n + up, (r + up) % ROUND, q, dma_ends[up])

            with nc.allow_non_contiguous_dma(reason="256 weights and 128 times a bias"):
                sp.dma_start(w1_cols[:, :], w1.rearrange("(h p) -> p h", p=P)).then_inc(w1_loaded, 16)
                sp.dma_start(neg_b1[:, :], b1.to_broadcast([P, 1])).then_inc(b1_loaded, 16)
            for c in range(SLOTS):
                if c == SLOTS - 1:
                    sp.wait_ge(w2_transposed, HALVES * HALVES)
                load(c // CHUNKS, c // CHUNKS, c % CHUNKS, c // CHUNKS * 16)
            stores_and_loads(0, 0, first=LAG)
            with sp.Fori(0, LAST // ROUND - 1) as i:
                for j in range(ROUND):
                    stores_and_loads(i * ROUND + (1 + j), (1 + j) % ROUND)
            for n in range(LAST - ROUND + 1, SAMPLES):
                stores_and_loads(n, n % ROUND, end=min(CHUNKS, TOTAL - SLOTS + LAG - n * CHUNKS))
            for k in range(CHUNKS):
                sp.wait_ge(chunk_stored[k], 16 * SAMPLES)

        @block.gpsimd
        def _(pool):
            nc.gpsimd.memset(identity, 0.0).then_inc(identity_zeroed, 1)
            pool.wait_ge(identity_zeroed, 1)
            nc.gpsimd.affine_select(out=identity, in_=identity, compare_op=ALU.not_equal, fill=1.0, base=0,
                                    pattern=[[-1, P]], channel_multiplier=1).then_inc(identity_made, 1)

        @block.tensor
        def _(pe):
            def transpose_w2():
                pe.wait_ge(w2_loaded, 16)
                pe.wait_ge(identity_made, 1)
                for ch in range(HALVES):
                    for oh in range(HALVES):
                        nc.tensor.transpose(transposed[:, ch, oh * P:(oh + 1) * P],
                                            w2_rows[:, oh, ch * P:(ch + 1) * P], identity).then_inc(w2_transposed, 1)

            def chunk_logits(n, r, k):
                pe.wait_ge(chunk_loaded[k], 16 * (n + 1))
                buf = (r * CHUNKS + k) % LOGIT_BUFS
                wait(pe, exp_ready, CHUNKS * n + k + 1 - LOGIT_BUFS)
                for b in range(CHUNK // BANK):
                    part = slice(b * BANK, (b + 1) * BANK)
                    for h in range(HALVES):
                        last = nc.tensor.matmul(logits[:, buf, part], neg_w1[:, h, :], xs[:, slot(r, k), h, part],
                                                start=(h == 0), stop=(h == HALVES - 1))
                last.then_inc(logits_ready, 1)

            def map_pooled(n, r):
                pe.wait_ge(w2_copied, 1)
                pe.wait_ge(pooled_ready, n + 1)
                wait(pe, context_ready, n)
                for oh in range(HALVES):
                    for ch in range(HALVES):
                        last = nc.tensor.matmul(mapped[:, oh:oh + 1], w2T[:, ch, oh * P:(oh + 1) * P],
                                                pooled[:, r, ch:ch + 1], start=(ch == 0), stop=(ch == HALVES - 1))
                last.then_inc(mapped_ready, 1)

            def body(n, r):
                for k in range(CHUNKS):
                    chunk_logits(n, r, k)
                    if k == 0 and isinstance(n, int):
                        transpose_w2()
                    elif k == 0:
                        map_pooled(n - 1, (r - 1) % ROUND)

            pe.wait_ge(w1_spread, HALVES)
            samples(pe, body)
            map_pooled(LAST, LAST % ROUND)

        @block.scalar
        def _(act):
            act.dma_start(w2_rows, w2.rearrange("(h p) c -> p h c", p=P)).then_inc(w2_loaded, 16)
            with nc.allow_non_contiguous_dma(reason="256 biases"):
                act.dma_start(b2_cols[:, :], b2.rearrange("(h p) -> p h", p=P)).then_inc(b2_loaded, 16)

            def chunk_exp(n, r, k):
                c = CHUNKS * n + k
                act.wait_ge(min_ready, c + 1)
                wait(act, chunk_pooled, c + 1 - EXP_BUFS)
                nc.scalar.activation(exps[:, k % EXP_BUFS, :], logits[:, (r * CHUNKS + k) % LOGIT_BUFS, :], ACT.Exp,
                                     bias=neg_max[:, r, k:k + 1], scale=-1.0,
                                     accum_out=sums[:, r, k:k + 1]).then_inc(exp_ready, 1)

            def chunk_weights(n, r):
                act.wait_ge(top_ready, n + 1)
                nc.scalar.activation(weights[:, r, :], neg_max[:, r, :], ACT.Exp, bias=neg_top[:, r:r + 1],
                                     scale=-1.0).then_inc(weights_ready, 1)

            def add_context(n, r, k):
                act.wait_ge(context_ready, n + 1)
                nc.scalar.activation(xs[:, slot(r, k), 0, :], xs[:, slot(r, k), 0, :], ACT.Identity,
                                     bias=context[:, r, 0:1], scale=1.0).then_inc(chunk_added[k], 1)

            def body(n, r):
                before = (r - 1) % ROUND
                first = isinstance(n, int)
                if not first:
                    chunk_weights(n - 1, before)
                for k in range(CHUNKS):
                    if not first:
                        add_context(n - 1, before, k)
                    chunk_exp(n, r, k)

            samples(act, body)
            chunk_weights(LAST, LAST % ROUND)
            for k in range(CHUNKS):
                add_context(LAST, LAST % ROUND, k)

        @block.vector
        def _(dve):
            nc.vector.memset(neg_w1[:, :, :], -1.0).then_inc(w1_ones, 1)
            dve.wait_ge(w1_ones, 1)
            dve.wait_ge(w1_loaded, 16)
            for h in range(HALVES):
                nc.vector.tensor_scalar(neg_w1[:, h, :], neg_w1[:, h, :], w1_cols[:, h:h + 1], None,
                                        ALU.mult).then_inc(w1_spread, 1)
            dve.wait_ge(b1_loaded, 16)
            nc.vector.tensor_scalar(neg_b1[:, :], neg_b1[:, :], -1.0, None, ALU.mult).then_inc(b1_negated, 1)
            dve.wait_ge(b1_negated, 1)

            def copy_w2T():
                dve.wait_ge(w2_transposed, HALVES * HALVES)
                nc.vector.tensor_copy(w2T[:, :, :], transposed[:, :, :]).then_inc(w2_copied, 1)

            def chunk_min(n, r, k):
                dve.wait_ge(logits_ready, CHUNKS * n + k + 1)
                y = logits[:, (r * CHUNKS + k) % LOGIT_BUFS, :]
                nc.vector.tensor_scalar(y, y, neg_b1[:, 0:1], None, ALU.add, ALU.min,
                                        accum_out=neg_max[:, r, k:k + 1]).then_inc(min_ready, 1)

            def chunk_pool(n, r, k):
                dve.wait_ge(exp_ready, CHUNKS * n + k + 1)
                for h in range(HALVES):
                    last = nc.vector.scalar_tensor_tensor(out=products[:, k % EXP_BUFS, h, :], in0=xs[:, slot(r, k), h, :], scalar=1.0,
                                                          in1=exps[:, k % EXP_BUFS, :], op0=ALU.mult, op1=ALU.mult,
                                                          accum_out=pools[:, r, h, k:k + 1])
                last.then_inc(chunk_pooled, 1)

            def finish_pool(n, r):
                nc.vector.tensor_reduce(out=neg_top[:, r:r + 1], in_=neg_max[:, r, :], axis=AX.X,
                                        op=ALU.min).then_inc(top_ready, 1)
                dve.wait_ge(weights_ready, n + 1)
                dve.wait_ge(chunk_pooled, CHUNKS * (n + 1))
                for h in range(HALVES):
                    last = nc.vector.scalar_tensor_tensor(out=weighted[:, h, :], in0=pools[:, r, h, :], scalar=1.0,
                                                          in1=weights[:, r, :], op0=ALU.mult, op1=ALU.mult,
                                                          accum_out=pooled[:, r, h:h + 1])
                last.then_inc(pooled_ready, 1)
                nc.vector.scalar_tensor_tensor(out=weighted[:, HALVES, :], in0=sums[:, r, :], scalar=1.0,
                                               in1=weights[:, r, :], op0=ALU.mult, op1=ALU.mult,
                                               accum_out=total[:, r:r + 1]).then_inc(total_ready, 1)
                dve.wait_ge(total_ready, n + 1)
                nc.vector.reciprocal(inverse[:, r:r + 1], total[:, r:r + 1]).then_inc(inverse_ready, 1)
                dve.wait_ge(inverse_ready, n + 1)
                dve.wait_ge(mapped_ready, n + 1)
                dve.wait_ge(b2_loaded, 16)
                nc.vector.scalar_tensor_tensor(out=context[:, r, :], in0=mapped[:, 0:HALVES],
                                               scalar=inverse[:, r:r + 1], in1=b2_cols[:, :], op0=ALU.mult,
                                               op1=ALU.add).then_inc(context_ready, 1)

            def add_context(n, r, k):
                dve.wait_ge(context_ready, n + 1)
                nc.vector.tensor_scalar(xs[:, slot(r, k), 1, :], xs[:, slot(r, k), 1, :], context[:, r, 1:2], None,
                                        ALU.add).then_inc(chunk_added[k], 1)

            def body(n, r):
                before = (r - 1) % ROUND
                first = isinstance(n, int)
                if not first:
                    chunk_pool(n - 1, before, CHUNKS - 1)
                    finish_pool(n - 1, before)
                for k in range(CHUNKS):
                    if not first:
                        add_context(n - 1, before, k)
                    chunk_min(n, r, k)
                    if k > 0:
                        chunk_pool(n, r, k - 1)
                    if first and k == 1:
                        copy_w2T()

            samples(dve, body)
            chunk_pool(LAST, LAST % ROUND, CHUNKS - 1)
            finish_pool(LAST, LAST % ROUND)
            for k in range(CHUNKS):
                add_context(LAST, LAST % ROUND, k)


_INS = ["x", "L0_conv_w1", "L0_conv_b1", "L0_conv_w2", "L0_conv_b2"]


def kernel(**inputs):
    import numpy as _np
    import concourse.bacc as _bacc
    from concourse import mybir as _mybir
    from concourse.bass_utils import run_bass_kernel_spmd as _run

    nc = _bacc.Bacc("TRN2", target_bir_lowering=False, num_devices=1,
                    dynamic_dma_scratch_size=1024)
    arrays, args = {}, []
    for name in _INS:
        a = _np.ascontiguousarray(inputs[name])
        if a.ndim == 0:
            a = a.reshape(1)
        arrays[f"in_{name}_dram"] = a
        args.append(nc.dram_tensor(f"in_{name}_dram", a.shape, _mybir.dt.from_np(a.dtype), kind="ExternalInput").ap())
    x = arrays["in_x_dram"]
    args.append(nc.dram_tensor("out_dram", x.shape, _mybir.dt.from_np(x.dtype), kind="ExternalOutput").ap())
    context_block_kernel(nc, *args)
    return _run(nc, [arrays], core_ids=[0]).results[0]["out_dram"]
```

```python
import concourse.bass as bass
from concourse import mybir
from contextlib import ExitStack


def context_block_kernel(nc: bass.Bass, x: bass.AP, w1: bass.AP, b1: bass.AP, w2: bass.AP, b2: bass.AP,
                         out: bass.AP):
    F32 = mybir.dt.float32
    ALU = mybir.AluOpType
    ACT = mybir.ActivationFunctionType
    AX = mybir.AxisListType

    P = 128
    SAMPLES, C, H, W = x.shape
    HALVES = C // P
    CHUNK = 1024
    CHUNKS = H * W // CHUNK
    SLOTS = 24
    BANK = 512
    LOGIT_BUFS = 3
    EXP_BUFS = 2
    ROUND = 3
    WARM_UPS = 12
    DONE = 16
    LAG = 2
    TOTAL = SAMPLES * CHUNKS
    LAST = SAMPLES - 1
    assert (ROUND * CHUNKS) % SLOTS == 0 and (ROUND * CHUNKS) % LOGIT_BUFS == 0
    assert CHUNKS % EXP_BUFS == 0 and LAST % ROUND == 0

    x_v = x.rearrange("n (h p) a b -> p n h (a b)", p=P)
    out_v = out.rearrange("n (h p) a b -> p n h (a b)", p=P)

    with ExitStack() as ctx:
        def sb(name, shape):
            return ctx.enter_context(nc.sbuf_tensor(name, shape, F32))

        def sem(name):
            return ctx.enter_context(nc.semaphore(name))

        xs = sb("xs", [P, SLOTS, HALVES, CHUNK])
        exps = sb("exps", [P, EXP_BUFS, CHUNK])
        products = sb("products", [P, EXP_BUFS, HALVES, CHUNK])
        w1_cols = sb("w1_cols", [P, HALVES])
        neg_w1 = sb("neg_w1", [P, HALVES, P])
        neg_b1 = sb("neg_b1", [P, 1])
        b2_cols = sb("b2_cols", [P, HALVES])
        w2T = sb("w2T", [P, HALVES, C])
        neg_max = sb("neg_max", [P, ROUND, CHUNKS])
        sums = sb("sums", [P, ROUND, CHUNKS])
        pools = sb("pools", [P, ROUND, HALVES, CHUNKS])
        neg_top = sb("neg_top", [P, ROUND])
        weights = sb("weights", [P, ROUND, CHUNKS])
        weighted = sb("weighted", [P, HALVES + 1, CHUNKS])
        total = sb("total", [P, ROUND])
        inverse = sb("inverse", [P, ROUND])
        pooled = sb("pooled", [P, ROUND, HALVES])
        context = sb("context", [P, ROUND, HALVES])
        w2_rows = xs[:, SLOTS - 1, 0, 0:HALVES * C].rearrange("p (h c) -> p h c", h=HALVES)
        identity = xs[:, SLOTS - 1, 1, 0:P]

        logits = ctx.enter_context(nc.psum_tensor("logits", [P, LOGIT_BUFS, CHUNK], F32))
        transposed = ctx.enter_context(nc.psum_tensor("transposed", [P, HALVES, C], F32))
        mapped = ctx.enter_context(nc.psum_tensor("mapped", [P, BANK], F32))

        first_bank_loaded = sem("first_bank_loaded")
        w1_loaded = sem("w1_loaded")
        b1_loaded = sem("b1_loaded")
        w2_loaded = sem("w2_loaded")
        b2_loaded = sem("b2_loaded")
        identity_zeroed = sem("identity_zeroed")
        identity_made = sem("identity_made")
        w1_spread = sem("w1_spread")
        w1_ones = sem("w1_ones")
        b1_negated = sem("b1_negated")
        w2_transposed = sem("w2_transposed")
        w2_copied = sem("w2_copied")
        chunk_loaded = [sem(f"chunk_loaded{k}") for k in range(CHUNKS)]
        chunk_stored = [sem(f"chunk_stored{k}") for k in range(CHUNKS)]
        logits_ready = sem("logits_ready")
        min_ready = sem("min_ready")
        exp_ready = sem("exp_ready")
        chunk_pooled = sem("chunk_pooled")
        top_ready = sem("top_ready")
        weights_ready = sem("weights_ready")
        total_ready = sem("total_ready")
        inverse_ready = sem("inverse_ready")
        pooled_ready = sem("pooled_ready")
        mapped_ready = sem("mapped_ready")
        context_ready = sem("context_ready")
        chunk_added = [sem(f"chunk_added{k}") for k in range(CHUNKS)]

        block = ctx.enter_context(nc.Block())

        def slot(r, k):
            return (r * CHUNKS + k) % SLOTS

        def wait(eng, semaphore, value):
            if not isinstance(value, int) or value > 0:
                eng.wait_ge(semaphore, value)

        def samples(eng, body):
            body(0, 0)
            with eng.Fori(0, LAST // ROUND) as i:
                for j in range(ROUND):
                    body(i * ROUND + (1 + j), (1 + j) % ROUND)

        @block.sync
        def _(sp):
            def work_out(value):
                if not isinstance(value, int):
                    sp.compute_val(value)
                return value

            def load(n, r, k, loads_before):
                wait(sp, chunk_loaded[k], loads_before)
                sp.dma_start(xs[:, slot(r, k)],
                             x_v[:, bass.ds(n, 1), :, k * CHUNK:(k + 1) * CHUNK]).then_inc(chunk_loaded[k], DONE)

            def stores_and_loads(n, r, first=0, end=CHUNKS):
                for m in range(3):
                    work_out((n + m) * (C * H * W) * 4)
                dma_ends = [work_out((n + m) * DONE) for m in range(3)]
                added = work_out((n + 1) * HALVES)
                for k in range(CHUNKS):
                    sp.wait_ge(chunk_added[k], added)
                    sp.dma_start(out_v[:, bass.ds(n, 1), :, k * CHUNK:(k + 1) * CHUNK],
                                 xs[:, slot(r, k)]).then_inc(chunk_stored[k], DONE)
                    if first <= k < end:
                        m, q = divmod(k - LAG, CHUNKS)
                        sp.wait_ge(chunk_stored[q], dma_ends[m + 1])
                        up, q = divmod(k - LAG + SLOTS, CHUNKS)
                        load(n + up, (r + up) % ROUND, q, dma_ends[up])

            with nc.allow_non_contiguous_dma(reason="256 weights and 128 times a bias"):
                sp.dma_start(w1_cols[:, :], w1.rearrange("(h p) -> p h", p=P)).then_inc(w1_loaded, DONE)
                sp.dma_start(neg_b1[:, :], b1.to_broadcast([P, 1])).then_inc(b1_loaded, DONE)
            sp.dma_start(xs[:, 0, :, 0:BANK], x_v[:, 0, :, 0:BANK]).then_inc(first_bank_loaded, DONE)
            sp.dma_start(xs[:, 0, :, BANK:CHUNK], x_v[:, 0, :, BANK:CHUNK]).then_inc(chunk_loaded[0], DONE)
            for c in range(1, SLOTS):
                if c == SLOTS - 1:
                    sp.wait_ge(w2_transposed, HALVES * HALVES)
                load(c // CHUNKS, c // CHUNKS, c % CHUNKS, c // CHUNKS * DONE)
            stores_and_loads(0, 0, first=LAG)
            with sp.Fori(0, LAST // ROUND - 1) as i:
                for j in range(ROUND):
                    stores_and_loads(i * ROUND + (1 + j), (1 + j) % ROUND)
            for n in range(LAST - ROUND + 1, SAMPLES):
                stores_and_loads(n, n % ROUND, end=min(CHUNKS, TOTAL - SLOTS + LAG - n * CHUNKS))
            for k in range(CHUNKS):
                sp.wait_ge(chunk_stored[k], DONE * SAMPLES)

        @block.gpsimd
        def _(pool):
            nc.gpsimd.memset(identity, 0.0).then_inc(identity_zeroed, 1)
            pool.wait_ge(identity_zeroed, 1)
            nc.gpsimd.affine_select(out=identity, in_=identity, compare_op=ALU.not_equal, fill=1.0, base=0,
                                    pattern=[[-1, P]], channel_multiplier=1).then_inc(identity_made, 1)

        @block.tensor
        def _(pe):
            def transpose_w2():
                pe.wait_ge(w2_loaded, DONE)
                pe.wait_ge(identity_made, 1)
                for ch in range(HALVES):
                    for oh in range(HALVES):
                        nc.tensor.transpose(transposed[:, ch, oh * P:(oh + 1) * P],
                                            w2_rows[:, oh, ch * P:(ch + 1) * P], identity).then_inc(w2_transposed, 1)

            def chunk_logits(n, r, k):
                if k > 0 or not isinstance(n, int):
                    pe.wait_ge(chunk_loaded[k], DONE * (n + 1))
                buf = (r * CHUNKS + k) % LOGIT_BUFS
                wait(pe, exp_ready, CHUNKS * n + k + 1 - LOGIT_BUFS)
                for b in range(CHUNK // BANK):
                    if k == 0 and isinstance(n, int):
                        pe.wait_ge(first_bank_loaded if b == 0 else chunk_loaded[0], DONE)
                    part = slice(b * BANK, (b + 1) * BANK)
                    for h in range(HALVES):
                        last = nc.tensor.matmul(logits[:, buf, part], neg_w1[:, h, :], xs[:, slot(r, k), h, part],
                                                start=(h == 0), stop=(h == HALVES - 1))
                last.then_inc(logits_ready, 1)

            def map_pooled(n, r):
                pe.wait_ge(w2_copied, 1)
                pe.wait_ge(pooled_ready, n + 1)
                for oh in range(HALVES):
                    for ch in range(HALVES):
                        last = nc.tensor.matmul(mapped[:, oh:oh + 1], w2T[:, ch, oh * P:(oh + 1) * P],
                                                pooled[:, r, ch:ch + 1], start=(ch == 0), stop=(ch == HALVES - 1))
                last.then_inc(mapped_ready, 1)

            def body(n, r):
                for k in range(CHUNKS):
                    chunk_logits(n, r, k)
                    if k == 0 and isinstance(n, int):
                        transpose_w2()
                    elif k == 0:
                        map_pooled(n - 1, (r - 1) % ROUND)

            pe.wait_ge(identity_made, 1)
            for _ in range(WARM_UPS):
                nc.tensor.matmul(mapped[:, 0:P], identity, identity, start=True, stop=True)
            pe.wait_ge(w1_spread, HALVES)
            samples(pe, body)
            map_pooled(LAST, LAST % ROUND)

        @block.scalar
        def _(act):
            act.dma_start(w2_rows, w2.rearrange("(h p) c -> p h c", p=P)).then_inc(w2_loaded, DONE)
            with nc.allow_non_contiguous_dma(reason="256 biases"):
                act.dma_start(b2_cols[:, :], b2.rearrange("(h p) -> p h", p=P)).then_inc(b2_loaded, DONE)

            def chunk_exp(n, r, k):
                c = CHUNKS * n + k
                act.wait_ge(min_ready, c + 1)
                wait(act, chunk_pooled, c + 1 - EXP_BUFS)
                nc.scalar.activation(exps[:, k % EXP_BUFS, :], logits[:, (r * CHUNKS + k) % LOGIT_BUFS, :], ACT.Exp,
                                     bias=neg_max[:, r, k:k + 1], scale=-1.0,
                                     accum_out=sums[:, r, k:k + 1]).then_inc(exp_ready, 1)

            def chunk_weights(n, r):
                act.wait_ge(top_ready, n + 1)
                nc.scalar.activation(weights[:, r, :], neg_max[:, r, :], ACT.Exp, bias=neg_top[:, r:r + 1],
                                     scale=-1.0).then_inc(weights_ready, 1)

            def add_context(n, r, k, halves=HALVES):
                act.wait_ge(context_ready, n + 1)
                for h in range(halves):
                    nc.scalar.activation(xs[:, slot(r, k), h, :], xs[:, slot(r, k), h, :], ACT.Identity,
                                         bias=context[:, r, h:h + 1], scale=1.0).then_inc(chunk_added[k], 1)

            def body(n, r):
                before = (r - 1) % ROUND
                first = isinstance(n, int)
                if not first:
                    chunk_weights(n - 1, before)
                for k in range(CHUNKS):
                    if not first:
                        add_context(n - 1, before, k)
                    chunk_exp(n, r, k)

            samples(act, body)
            chunk_weights(LAST, LAST % ROUND)
            for k in range(CHUNKS):
                add_context(LAST, LAST % ROUND, k, halves=HALVES - 1)

        @block.vector
        def _(dve):
            nc.vector.memset(neg_w1[:, :, :], -1.0).then_inc(w1_ones, 1)
            dve.wait_ge(w1_ones, 1)
            dve.wait_ge(w1_loaded, DONE)
            for h in range(HALVES):
                nc.vector.tensor_scalar(neg_w1[:, h, :], neg_w1[:, h, :], w1_cols[:, h:h + 1], None,
                                        ALU.mult).then_inc(w1_spread, 1)
            dve.wait_ge(b1_loaded, DONE)
            nc.vector.tensor_scalar(neg_b1[:, :], neg_b1[:, :], -1.0, None, ALU.mult).then_inc(b1_negated, 1)
            dve.wait_ge(b1_negated, 1)

            def copy_w2T():
                dve.wait_ge(w2_transposed, HALVES * HALVES)
                nc.vector.tensor_copy(w2T[:, :, :], transposed[:, :, :]).then_inc(w2_copied, 1)

            def chunk_min(n, r, k):
                dve.wait_ge(logits_ready, CHUNKS * n + k + 1)
                y = logits[:, (r * CHUNKS + k) % LOGIT_BUFS, :]
                nc.vector.tensor_scalar(y, y, neg_b1[:, 0:1], None, ALU.add, ALU.min,
                                        accum_out=neg_max[:, r, k:k + 1]).then_inc(min_ready, 1)

            def chunk_pool(n, r, k):
                dve.wait_ge(exp_ready, CHUNKS * n + k + 1)
                for h in range(HALVES):
                    last = nc.vector.scalar_tensor_tensor(out=products[:, k % EXP_BUFS, h, :],
                                                          in0=xs[:, slot(r, k), h, :], scalar=1.0,
                                                          in1=exps[:, k % EXP_BUFS, :], op0=ALU.mult, op1=ALU.mult,
                                                          accum_out=pools[:, r, h, k:k + 1])
                last.then_inc(chunk_pooled, 1)

            def finish_pool(n, r):
                nc.vector.tensor_reduce(out=neg_top[:, r:r + 1], in_=neg_max[:, r, :], axis=AX.X,
                                        op=ALU.min).then_inc(top_ready, 1)
                dve.wait_ge(weights_ready, n + 1)
                dve.wait_ge(chunk_pooled, CHUNKS * (n + 1))
                for h in range(HALVES):
                    last = nc.vector.scalar_tensor_tensor(out=weighted[:, h, :], in0=pools[:, r, h, :], scalar=1.0,
                                                          in1=weights[:, r, :], op0=ALU.mult, op1=ALU.mult,
                                                          accum_out=pooled[:, r, h:h + 1])
                last.then_inc(pooled_ready, 1)
                nc.vector.scalar_tensor_tensor(out=weighted[:, HALVES, :], in0=sums[:, r, :], scalar=1.0,
                                               in1=weights[:, r, :], op0=ALU.mult, op1=ALU.mult,
                                               accum_out=total[:, r:r + 1]).then_inc(total_ready, 1)
                dve.wait_ge(total_ready, n + 1)
                nc.vector.reciprocal(inverse[:, r:r + 1], total[:, r:r + 1]).then_inc(inverse_ready, 1)
                dve.wait_ge(inverse_ready, n + 1)
                dve.wait_ge(mapped_ready, n + 1)
                dve.wait_ge(b2_loaded, DONE)
                nc.vector.scalar_tensor_tensor(out=context[:, r, :], in0=mapped[:, 0:HALVES],
                                               scalar=inverse[:, r:r + 1], in1=b2_cols[:, :], op0=ALU.mult,
                                               op1=ALU.add).then_inc(context_ready, 1)

            def add_context(n, r, k):
                dve.wait_ge(context_ready, n + 1)
                nc.vector.tensor_scalar(xs[:, slot(r, k), 1, :], xs[:, slot(r, k), 1, :], context[:, r, 1:2], None,
                                        ALU.add).then_inc(chunk_added[k], 1)

            def body(n, r):
                before = (r - 1) % ROUND
                first = isinstance(n, int)
                if not first:
                    chunk_pool(n - 1, before, CHUNKS - 1)
                    finish_pool(n - 1, before)
                for k in range(CHUNKS):
                    chunk_min(n, r, k)
                    if k > 0:
                        chunk_pool(n, r, k - 1)
                    if first and k == 1:
                        copy_w2T()

            samples(dve, body)
            chunk_pool(LAST, LAST % ROUND, CHUNKS - 1)
            finish_pool(LAST, LAST % ROUND)
            for k in range(CHUNKS):
                add_context(LAST, LAST % ROUND, k)


_INS = ["x", "L0_conv_w1", "L0_conv_b1", "L0_conv_w2", "L0_conv_b2"]


def kernel(**inputs):
    import numpy as _np
    import concourse.bacc as _bacc
    from concourse import mybir as _mybir
    from concourse.bass_utils import run_bass_kernel_spmd as _run

    nc = _bacc.Bacc("TRN2", target_bir_lowering=False, num_devices=1,
                    dynamic_dma_scratch_size=1024)
    arrays, args = {}, []
    for name in _INS:
        a = _np.ascontiguousarray(inputs[name])
        if a.ndim == 0:
            a = a.reshape(1)
        arrays[f"in_{name}_dram"] = a
        args.append(nc.dram_tensor(f"in_{name}_dram", a.shape, _mybir.dt.from_np(a.dtype), kind="ExternalInput").ap())
    x = arrays["in_x_dram"]
    args.append(nc.dram_tensor("out_dram", x.shape, _mybir.dt.from_np(x.dtype), kind="ExternalOutput").ap())
    context_block_kernel(nc, *args)
    return _run(nc, [arrays], core_ids=[0]).results[0]["out_dram"]
```
